# Optimizing a Trainium2 kernel written in Bass

```python
import numpy as np
import jax
import jax.numpy as jnp

def _softmax(x, axis=-1):
    return jax.nn.softmax(x, axis=axis)

def _gelu(x):
    return jax.nn.gelu(x, approximate=True)

def _silu(x):
    return jax.nn.silu(x)

def _sigmoid(x):
    return jax.nn.sigmoid(x)

def _layernorm(x, axis=-1, eps=1e-05):
    m = jnp.mean(x, axis=axis, keepdims=True)
    v = jnp.var(x, axis=axis, keepdims=True)
    return (x - m) / jnp.sqrt(v + eps)

def _scatter_add(tgt, idx, src, axis=0):
    return tgt.at[idx].add(src)

def _segment_sum(src, seg, n):
    return jax.ops.segment_sum(src, seg, n)
kernel_name = 'mk_dlrm_tower_d1_rec_r8_9914cb'

def setup_inputs(seed: int=0):
    np.random.seed(seed)
    _w = jnp.asarray

    def _rec_inputs():
        import jax
        import jax.numpy as jnp
        _tk = jax.random.key(seed)
        ids = jnp.stack([jax.random.randint(jax.random.fold_in(_tk, 200 + f), (512,), 0, v, jnp.int32) for f, v in enumerate([1250, 12500, 1250, 1000, 1250, 1250, 125000, 12500, 1250, 1000, 1000, 1250, 1000, 12500, 12500, 12500, 12500, 1250, 12500, 12500, 1250, 1250, 1000, 1250, 1250, 1000])], axis=1)
        tbl_0 = 0.05 * jax.random.normal(jax.random.fold_in(_tk, 500 + 0), (1250, 128), jnp.float32)
        tbl_1 = 0.05 * jax.random.normal(jax.random.fold_in(_tk, 500 + 1), (12500, 128), jnp.float32)
        tbl_2 = 0.05 * jax.random.normal(jax.random.fold_in(_tk, 500 + 2), (1250, 128), jnp.float32)
        tbl_3 = 0.05 * jax.random.normal(jax.random.fold_in(_tk, 500 + 3), (1000, 128), jnp.float32)
        tbl_4 = 0.05 * jax.random.normal(jax.random.fold_in(_tk, 500 + 4), (1250, 128), jnp.float32)
        tbl_5 = 0.05 * jax.random.normal(jax.random.fold_in(_tk, 500 + 5), (1250, 128), jnp.float32)
        tbl_6 = 0.05 * jax.random.normal(jax.random.fold_in(_tk, 500 + 6), (125000, 128), jnp.float32)
        tbl_7 = 0.05 * jax.random.normal(jax.random.fold_in(_tk, 500 + 7), (12500, 128), jnp.float32)
        tbl_8 = 0.05 * jax.random.normal(jax.random.fold_in(_tk, 500 + 8), (1250, 128), jnp.float32)
        tbl_9 = 0.05 * jax.random.normal(jax.random.fold_in(_tk, 500 + 9), (1000, 128), jnp.float32)
        tbl_10 = 0.05 * jax.random.normal(jax.random.fold_in(_tk, 500 + 10), (1000, 128), jnp.float32)
        tbl_11 = 0.05 * jax.random.normal(jax.random.fold_in(_tk, 500 + 11), (1250, 128), jnp.float32)
        tbl_12 = 0.05 * jax.random.normal(jax.random.fold_in(_tk, 500 + 12), (1000, 128), jnp.float32)
        tbl_13 = 0.05 * jax.random.normal(jax.random.fold_in(_tk, 500 + 13), (12500, 128), jnp.float32)
        tbl_14 = 0.05 * jax.random.normal(jax.random.fold_in(_tk, 500 + 14), (12500, 128), jnp.float32)
        tbl_15 = 0.05 * jax.random.normal(jax.random.fold_in(_tk, 500 + 15), (12500, 128), jnp.float32)
        tbl_16 = 0.05 * jax.random.normal(jax.random.fold_in(_tk, 500 + 16), (12500, 128), jnp.float32)
        tbl_17 = 0.05 * jax.random.normal(jax.random.fold_in(_tk, 500 + 17), (1250, 128), jnp.float32)
        tbl_18 = 0.05 * jax.random.normal(jax.random.fold_in(_tk, 500 + 18), (12500, 128), jnp.float32)
        tbl_19 = 0.05 * jax.random.normal(jax.random.fold_in(_tk, 500 + 19), (12500, 128), jnp.float32)
        tbl_20 = 0.05 * jax.random.normal(jax.random.fold_in(_tk, 500 + 20), (1250, 128), jnp.float32)
        tbl_21 = 0.05 * jax.random.normal(jax.random.fold_in(_tk, 500 + 21), (1250, 128), jnp.float32)
        tbl_22 = 0.05 * jax.random.normal(jax.random.fold_in(_tk, 500 + 22), (1000, 128), jnp.float32)
        tbl_23 = 0.05 * jax.random.normal(jax.random.fold_in(_tk, 500 + 23), (1250, 128), jnp.float32)
        tbl_24 = 0.05 * jax.random.normal(jax.random.fold_in(_tk, 500 + 24), (1250, 128), jnp.float32)
        tbl_25 = 0.05 * jax.random.normal(jax.random.fold_in(_tk, 500 + 25), (1000, 128), jnp.float32)
        _rk = jax.random.fold_in(_tk, 7)
        r_dense_x = -0.000514642 + 1.00011 * jax.random.normal(jax.random.fold_in(_rk, 101), (512, 128), jnp.float32)
        W_top1 = 0.0456912 * jax.random.normal(jax.random.fold_in(_tk, 801), (479, 512), jnp.float32)
        W_top2 = 0.0441942 * jax.random.normal(jax.random.fold_in(_tk, 802), (512, 256), jnp.float32)
        W_top3 = 0.0625 * jax.random.normal(jax.random.fold_in(_tk, 803), (256, 1), jnp.float32)
        b_top1 = jnp.zeros((512,), jnp.float32)
        b_top2 = jnp.zeros((256,), jnp.float32)
        return (r_dense_x, ids, tbl_0, tbl_1, tbl_2, tbl_3, tbl_4, tbl_5, tbl_6, tbl_7, tbl_8, tbl_9, tbl_10, tbl_11, tbl_12, tbl_13, tbl_14, tbl_15, tbl_16, tbl_17, tbl_18, tbl_19, tbl_20, tbl_21, tbl_22, tbl_23, tbl_24, tbl_25, W_top1, b_top1, W_top2, b_top2, W_top3)
    r_dense_x, ids, tbl_0, tbl_1, tbl_2, tbl_3, tbl_4, tbl_5, tbl_6, tbl_7, tbl_8, tbl_9, tbl_10, tbl_11, tbl_12, tbl_13, tbl_14, tbl_15, tbl_16, tbl_17, tbl_18, tbl_19, tbl_20, tbl_21, tbl_22, tbl_23, tbl_24, tbl_25, W_top1, b_top1, W_top2, b_top2, W_top3 = _rec_inputs()

    def _L0_rec_setup():
        import jax, jax.numpy as jnp
        import numpy as np
        F = 26
        D = 128
        B = 2048
        _TRIU_I, _TRIU_J = np.triu_indices(F + 1, k=1)
        _TRIU_I = jnp.asarray(_TRIU_I)
        _TRIU_J = jnp.asarray(_TRIU_J)
        key = jax.random.key(seed)
        k1, k2 = jax.random.split(key)
        sparse_x = jax.random.normal(k1, (B, F, D), dtype=jnp.float32)
        dense_x = jax.random.normal(k2, (B, D), dtype=jnp.float32)
        return {'sparse_x': sparse_x, 'dense_x': dense_x}
    _L0_rec_all = _L0_rec_setup()
    _L0_rec_in = {k: v for k, v in _L0_rec_all.items() if k in ()}
    del _L0_rec_all
    return {'r_dense_x': r_dense_x, 'ids': ids, 'tbl_0': tbl_0, 'tbl_1': tbl_1, 'tbl_2': tbl_2, 'tbl_3': tbl_3, 'tbl_4': tbl_4, 'tbl_5': tbl_5, 'tbl_6': tbl_6, 'tbl_7': tbl_7, 'tbl_8': tbl_8, 'tbl_9': tbl_9, 'tbl_10': tbl_10, 'tbl_11': tbl_11, 'tbl_12': tbl_12, 'tbl_13': tbl_13, 'tbl_14': tbl_14, 'tbl_15': tbl_15, 'tbl_16': tbl_16, 'tbl_17': tbl_17, 'tbl_18': tbl_18, 'tbl_19': tbl_19, 'tbl_20': tbl_20, 'tbl_21': tbl_21, 'tbl_22': tbl_22, 'tbl_23': tbl_23, 'tbl_24': tbl_24, 'tbl_25': tbl_25, 'W_top1': W_top1, 'b_top1': b_top1, 'W_top2': W_top2, 'b_top2': b_top2, 'W_top3': W_top3}

def reference(r_dense_x, ids, tbl_0, tbl_1, tbl_2, tbl_3, tbl_4, tbl_5, tbl_6, tbl_7, tbl_8, tbl_9, tbl_10, tbl_11, tbl_12, tbl_13, tbl_14, tbl_15, tbl_16, tbl_17, tbl_18, tbl_19, tbl_20, tbl_21, tbl_22, tbl_23, tbl_24, tbl_25, W_top1, b_top1, W_top2, b_top2, W_top3):
    import jax
    import jax.numpy as jnp

    def _L0_rec_ref(sparse_x, dense_x):
        import jax, jax.numpy as jnp
        import numpy as np
        F = 26
        D = 128
        B = 2048
        _TRIU_I, _TRIU_J = np.triu_indices(F + 1, k=1)
        _TRIU_I = jnp.asarray(_TRIU_I)
        _TRIU_J = jnp.asarray(_TRIU_J)
        combined = jnp.concatenate([sparse_x, dense_x[:, None, :]], axis=1)
        interact = jnp.einsum('bfd,bgd->bfg', combined, combined)
        return interact[:, _TRIU_I, _TRIU_J]
    e = jnp.stack([tbl_0[ids[:, 0]], tbl_1[ids[:, 1]], tbl_2[ids[:, 2]], tbl_3[ids[:, 3]], tbl_4[ids[:, 4]], tbl_5[ids[:, 5]], tbl_6[ids[:, 6]], tbl_7[ids[:, 7]], tbl_8[ids[:, 8]], tbl_9[ids[:, 9]], tbl_10[ids[:, 10]], tbl_11[ids[:, 11]], tbl_12[ids[:, 12]], tbl_13[ids[:, 13]], tbl_14[ids[:, 14]], tbl_15[ids[:, 15]], tbl_16[ids[:, 16]], tbl_17[ids[:, 17]], tbl_18[ids[:, 18]], tbl_19[ids[:, 19]], tbl_20[ids[:, 20]], tbl_21[ids[:, 21]], tbl_22[ids[:, 22]], tbl_23[ids[:, 23]], tbl_24[ids[:, 24]], tbl_25[ids[:, 25]]], axis=1)
    z = _L0_rec_ref(e, r_dense_x)
    z = z.reshape(z.shape[0], -1)
    h = jnp.concatenate([z, r_dense_x], axis=1)
    h = jnp.maximum(h @ W_top1 + b_top1, 0.0)
    h = jnp.maximum(h @ W_top2 + b_top2, 0.0)
    y = h @ W_top3
    return y

_drawn_inputs = setup_inputs


def setup_inputs(seed=0):
    import zlib

    import numpy as np

    out = dict(_drawn_inputs(seed))
    spreads = {'b_top1': (0.0, 0.1), 'b_top2': (0.0, 0.1)}
    factors = {}
    for name, (base, spread) in spreads.items():
        noise = np.random.default_rng([zlib.crc32(name.encode()), seed]).standard_normal(out[name].shape)
        drawn = base * np.exp(spread * noise) if base else spread * noise
        out[name] = jnp.asarray(drawn.astype(out[name].dtype))
    for name, factor in factors.items():
        out[name] = (out[name] * factor).astype(out[name].dtype)
    return out
```

```python
from contextlib import ExitStack

import concourse.bass as bass
from concourse import mybir

F32 = mybir.dt.float32
I32 = mybir.dt.int32
ALU = mybir.AluOpType
ACT = mybir.ActivationFunctionType

P = 128
TILES = 4
BATCH = TILES * P
FIELDS = 26
SLOTS = FIELDS + 1
D = 128
VOCAB = [1250, 12500, 1250, 1000, 1250, 1250, 125000, 12500, 1250, 1000, 1000, 1250, 1000,
         12500, 12500, 12500, 12500, 1250, 12500, 12500, 1250, 1250, 1000, 1250, 1250, 1000]

ONEHOT_FIELDS = [3, 9, 10, 12, 22, 25]
GATHER_FIELDS = [f for f in range(FIELDS) if f not in ONEHOT_FIELDS]
SLOT_FIELDS = ONEHOT_FIELDS + GATHER_FIELDS + [FIELDS]
NO = len(ONEHOT_FIELDS)
NG = len(GATHER_FIELDS)
DENSE = SLOTS - 1

ROWS = 125
CHUNKS = [VOCAB[f] // ROWS for f in ONEHOT_FIELDS]
CHUNK0 = [sum(CHUNKS[:i]) for i in range(NO)]

PER_BANK = 4
RAW_GROUPS = [range(i, min(i + PER_BANK, NG)) for i in range(0, NG, PER_BANK)]
HALF_GROUPS = (len(RAW_GROUPS) + 1) // 2
HALF = HALF_GROUPS * PER_BANK
PAIR_GROUPS = [range(i, min(i + PER_BANK, SLOTS)) for i in range(1, SLOTS, PER_BANK)]
PAIRS = SLOTS * (SLOTS - 1) // 2
PAIR_CHUNKS = -(-PAIRS // P)
USES = len(RAW_GROUPS) + len(PAIR_GROUPS)
RAW_A, RAW_B = -(-len(RAW_GROUPS) // 2), len(RAW_GROUPS) // 2
JQ = P // 4
QB = JQ // 2
H1 = 512
H2 = 256
N1 = H1 // P
N2 = H2 // P


def pair_at(f, g):
    return g * (g - 1) // 2 + f


def build(nc, ids_gather, ids_onehot, x, tables, w1, b1, w2, b2, w3, out):
    with ExitStack() as ctx:
        def sb(name, shape, dt=F32):
            return ctx.enter_context(nc.sbuf_tensor(name, shape, dt))

        def sem(name):
            return ctx.enter_context(nc.semaphore(name))

        ident = sb("ident", [P, P])
        zeros = sb("zeros", [P, QB * SLOTS])
        row_ids = sb("row_ids", [P, 2, 10])
        ids_now = sb("ids_now", [P, NG], I32)
        ids_wide = sb("ids_wide", [P, NO, BATCH], I32)
        table = sb("table", [P, sum(CHUNKS), D])
        onehot = sb("onehot", [P, sum(CHUNKS), BATCH])
        rows = sb("rows", [P, NG, D])
        x_rows = sb("x_rows", [P, TILES, D])
        x_t = sb("x_t", [P, BATCH])
        vecs = sb("vecs", [P, P, 32])
        gram = sb("gram", [P, SLOTS, JQ])
        pairs = sb("pairs", [JQ, 4, PAIR_CHUNKS * P])
        pairs_t = sb("pairs_t", [P, PAIR_CHUNKS, P])
        w1_sb = sb("w1_sb", [P, PAIR_CHUNKS + 1, H1])
        w2_sb = sb("w2_sb", [P, N1, H2])
        w3_sb = sb("w3_sb", [P, N2])
        b1_sb = sb("b1_sb", [P, N1])
        b2_sb = sb("b2_sb", [P, N2])
        h1 = sb("h1", [P, N1, P])
        h2 = sb("h2", [P, N2, P])
        y = sb("y", [1, BATCH])

        turn_ps = ctx.enter_context(nc.psum_tensor("turn_ps", [P, 2, 512], F32))
        look_ps = ctx.enter_context(nc.psum_tensor("look_ps", [P, 2, 512], F32))
        gram_ps = ctx.enter_context(nc.psum_tensor("gram_ps", [P, 2, 512], F32))
        mlp_ps = ctx.enter_context(nc.psum_tensor("mlp_ps", [P, 2, 512], F32))

        ids_landed = [sem("ids_landed_a"), sem("ids_landed_b")]
        wide_landed = sem("wide_landed")
        x_landed = sem("x_landed")
        table_landed = [sem(f"table_landed{i}") for i in range(NO)]
        w1_landed, w2_landed, small_landed = sem("w1_landed"), sem("w2_landed"), sem("small_landed")
        rows_landed = [sem(f"rows_landed{g}") for g in range(len(RAW_GROUPS))]
        group_begun = sem("group_begun")
        blank = sem("blank")
        consts_ready = sem("consts_ready")
        zeros_ready = sem("zeros_ready")
        onehot_ready = sem("onehot_ready")
        wiped = sem("wiped")
        turned = sem("turned")
        turn_saved = [sem("turn_saved_dve"), sem("turn_saved_act")]
        looked = [sem("looked_a"), sem("looked_b")]
        look_saved = [sem("look_saved_dve"), sem("look_saved_act")]
        gram_done = [sem("gram_done_a"), sem("gram_done_b")]
        gram_saved = [sem("gram_saved_dve"), sem("gram_saved_act")]
        x_placed = sem("x_placed")
        pairs_turned = sem("pairs_turned")
        pairs_saved = [sem("pairs_saved_dve"), sem("pairs_saved_act")]
        h1_done = sem("h1_done")
        h1_saved = [sem("h1_saved_dve"), sem("h1_saved_act")]
        h2_done = sem("h2_done")
        h2_saved = [sem("h2_saved_dve"), sem("h2_saved_act")]
        y_done = sem("y_done")
        y_saved = sem("y_saved")
        out_landed = sem("out_landed")

        ids_tiles = ids_gather.rearrange("(t p) f -> t p f", p=P)
        halves = [slice(0, HALF), slice(HALF, NG)]
        half_groups = [range(HALF_GROUPS), range(HALF_GROUPS, len(RAW_GROUPS))]

        block = ctx.enter_context(nc.Block())

        @block.sync
        def _(sp):
            for h in range(2):
                sp.dma_start(ids_now[:, halves[h]], ids_tiles[0, :, halves[h]]).then_inc(ids_landed[h], 16)
            sp.dma_start(x_rows[:], x.rearrange("(t p) d -> p t d", p=P)).then_inc(x_landed, 16)
            for i in range(1, NO, 2):
                sp.dma_start(table[0:ROWS, CHUNK0[i]:CHUNK0[i] + CHUNKS[i], :],
                             tables[ONEHOT_FIELDS[i]].rearrange("(p k) d -> p k d", p=ROWS)
                             ).then_inc(table_landed[i], 16)
            with sp.Fori(0, TILES - 1) as t:
                for h in range(2):
                    for g in half_groups[h]:
                        sp.wait_ge(rows_landed[g], t * (16 * len(RAW_GROUPS[g])) + 16 * len(RAW_GROUPS[g]))
                    sp.dma_start(ids_now[:, halves[h]], ids_tiles[t + 1, :, halves[h]]
                                 ).then_inc(ids_landed[h], 16)
            sp.wait_ge(y_saved, TILES)
            sp.dma_start(out.rearrange("b o -> o b"), y[:]).then_inc(out_landed, 16)
            sp.wait_ge(out_landed, 16)

        @block.gpsimd
        def _(pool):
            nc.gpsimd.memset(ident[:], 0.0).then_inc(blank, 1)
            pool.wait_ge(blank, 1)
            nc.gpsimd.affine_select(out=ident[:], in_=ident[:], compare_op=ALU.not_equal, fill=1.0, base=0,
                                    pattern=[[-1, P]], channel_multiplier=1).then_inc(consts_ready, 1)
            for i, n in enumerate((8, 10)):
                nc.gpsimd.iota(row_ids[:, i, 0:n], pattern=[[1, n]], base=0, channel_multiplier=n,
                               allow_small_or_imprecise_dtypes=True).then_inc(consts_ready, 1)

            def gather_tile(t, first):
                for h in range(2):
                    pool.wait_ge(ids_landed[h], t * 16 + 16)
                    for g in half_groups[h]:
                        if not first:
                            pool.wait_ge(turned, t * USES + (2 - USES + g + 1))
                            pool.sem_inc(group_begun, 1)
                        for i in RAW_GROUPS[g]:
                            nc.gpsimd.indirect_dma_start(
                                rows[:, i, :], None, tables[GATHER_FIELDS[i]],
                                bass.IndirectOffsetOnAxis(ap=ids_now[:, i:i + 1], axis=0)
                            ).then_inc(rows_landed[g], 16)

            gather_tile(0, True)
            with pool.Fori(1, TILES) as t:
                gather_tile(t, False)

        def slots_of(group):
            return slice(NO + group[0], NO + group[-1] + 1)

        def spread(bank, n):
            return bank[:, 0:n * P].rearrange("p (s b) -> p b s", b=P)

        @block.tensor
        def _(pe):
            def turn_free(t, u):
                pe.wait_ge(turn_saved[u % 2], t * (USES // 2) + (u // 2 + 1))

            def look_up(t, i):
                bank, at = divmod(i, PER_BANK)
                for k in range(CHUNKS[i]):
                    mm = nc.tensor.matmul(look_ps[:, bank, at * P:(at + 1) * P],
                                          table[0:ROWS, CHUNK0[i] + k, :],
                                          onehot[0:ROWS, CHUNK0[i] + k, bass.ts(t, P)],
                                          start=(k == 0), stop=(k == CHUNKS[i] - 1))
                if i in (PER_BANK - 1, NO - 1):
                    mm.then_inc(looked[bank], 1)

            def look_ups(t, those):
                for i in those:
                    if i % PER_BANK == 0:
                        pe.wait_ge(look_saved[i // PER_BANK], t + 1)
                    look_up(t + 1, i)

            pe.wait_ge(zeros_ready, 1)
            for b in range(2):
                nc.tensor.matmul(gram_ps[:, b, 0:QB * SLOTS], zeros[:, 0:P], zeros[:, :], start=True,
                                 stop=True).then_inc(wiped, 1)
            pe.wait_ge(consts_ready, 1)
            pe.wait_ge(x_landed, 16)
            for b in range(2):
                for i in range(2):
                    mm = nc.tensor.transpose(turn_ps[:, b, i * P:(i + 1) * P], x_rows[:, 2 * b + i, :], ident[:])
                mm.then_inc(turned, 1)
            for i in range(NO):
                pe.wait_ge(table_landed[i], 16)
                pe.wait_ge(onehot_ready, i + 1)
                look_up(0, i)

            def tile(t, last):
                for u, group in enumerate(RAW_GROUPS):
                    turn_free(t, u)
                    pe.wait_ge(rows_landed[u], t * (16 * len(group)) + 16 * len(group))
                    for n, i in enumerate(group):
                        mm = nc.tensor.transpose(turn_ps[:, u % 2, n * P:(n + 1) * P], rows[:, i, :], ident[:])
                    mm.then_inc(turned, 1)
                pe.wait_ge(turn_saved[0], t * (USES // 2) + RAW_A + 1)
                pe.wait_ge(turn_saved[1], t * (USES // 2) + RAW_B + 1)
                for b in range(2):
                    pe.wait_ge(look_saved[b], t + 1)
                pe.wait_ge(x_placed, t + 1)
                for b in range(2):
                    for q in range(QB):
                        for j in range(4):
                            v = vecs[:, j * JQ + b * QB + q, 0:SLOTS]
                            mm = nc.tensor.matmul(gram_ps[32 * j:32 * j + SLOTS, b, q * SLOTS:(q + 1) * SLOTS],
                                                  v, v, start=True, stop=True)
                    mm.then_inc(gram_done[b], 1)
                if not last:
                    look_ups(t, [0, 1])
                if last is not None:
                    pass
                for n in range(N1):
                    nc.tensor.matmul(mlp_ps[:, n // 2, (n % 2) * P:(n % 2 + 1) * P],
                                     w1_sb[:, PAIR_CHUNKS, n * P:(n + 1) * P], x_t[:, bass.ts(t, P)],
                                     start=(n % 2 == 0), stop=False, skip_group_check=True)
                for b in range(2):
                    pe.wait_ge(gram_saved[b], t + 1)
                for a, group in enumerate(PAIR_GROUPS):
                    u = len(RAW_GROUPS) + a
                    turn_free(t, u)
                    for n, g in enumerate(group):
                        mm = nc.tensor.transpose(turn_ps[0:JQ, u % 2, n * P:(n + 1) * P], gram[:, g, :], ident[:])
                    mm.then_inc(turned, 1)
                if not last:
                    look_ups(t, [2])
                for b in range(2):
                    pe.wait_ge(turn_saved[b], t * (USES // 2) + USES // 2 + 1)
                for j in range(4):
                    for c in range(PAIR_CHUNKS):
                        at = (j % 2) * PAIR_CHUNKS * JQ + c * JQ
                        mm = nc.tensor.matmul(gram_ps[:, j // 2, at:at + JQ], pairs[:, j, c * P:(c + 1) * P],
                                              ident[0:JQ, 0:JQ], start=True, stop=True)
                mm.then_inc(pairs_turned, 1)
                if not last:
                    look_ups(t, [3])
                for b in range(2):
                    pe.wait_ge(pairs_saved[b], t + 1)
                for n in range(N1):
                    for c in range(PAIR_CHUNKS):
                        mm = nc.tensor.matmul(mlp_ps[:, n // 2, (n % 2) * P:(n % 2 + 1) * P],
                                              w1_sb[:, c, n * P:(n + 1) * P], pairs_t[:, c, :], start=False,
                                              stop=(c == PAIR_CHUNKS - 1), skip_group_check=True)
                mm.then_inc(h1_done, 1)
                if not last:
                    look_ups(t, [4])
                for b in range(2):
                    pe.wait_ge(h1_saved[b], t + 1)
                for m in range(N2):
                    for n in range(N1):
                        mm = nc.tensor.matmul(mlp_ps[:, m, 2 * P:3 * P], w2_sb[:, n, m * P:(m + 1) * P],
                                              h1[:, n, :], start=(n == 0), stop=(n == N1 - 1))
                mm.then_inc(h2_done, 1)
                if not last:
                    look_ups(t, [5])
                for b in range(2):
                    pe.wait_ge(h2_saved[b], t + 1)
                for m in range(N2):
                    mm = nc.tensor.matmul(mlp_ps[0:1, 0, 3 * P:4 * P], w3_sb[:, m:m + 1], h2[:, m, :],
                                          start=(m == 0), stop=(m == N2 - 1))
                mm.then_inc(y_done, 1)
                if not last:
                    pe.wait_ge(y_saved, t + 1)

            pe.wait_ge(w1_landed, 16)
            pe.wait_ge(w2_landed, 16)
            pe.wait_ge(small_landed, 48)
            with pe.Fori(0, TILES - 1) as t:
                tile(t, False)
            tile(TILES - 1, True)

        def pack(copy, t, u):
            for n, g in enumerate(PAIR_GROUPS[u - len(RAW_GROUPS)]):
                src = turn_ps[0:JQ, u % 2, n * P:(n + 1) * P].rearrange("q (j f) -> q j f", j=4)[:, :, 0:g]
                last = copy(pairs[:, :, pair_at(0, g):pair_at(0, g) + g], src)
            return last

        @block.vector
        def _(dve):
            copy = nc.vector.tensor_copy
            nc.vector.memset(zeros[:], 0.0).then_inc(zeros_ready, 1)
            nc.vector.memset(pairs[:, :, PAIRS:], 0.0)
            dve.wait_ge(consts_ready, 3)
            dve.wait_ge(wide_landed, 16)
            for i in range(NO):
                for k in range(CHUNKS[i]):
                    last = nc.vector.tensor_scalar(onehot[:, CHUNK0[i] + k, :], ids_wide[:, i, :],
                                                   row_ids[:, (CHUNKS[i] - 8) // 2, k:k + 1], None, ALU.is_equal)
                last.then_inc(onehot_ready, 1)
                if i == 0:
                    dve.wait_ge(turned, 1)
                    copy(x_t[:, 0:2 * P], turn_ps[:, 0, 0:2 * P]).then_inc(turn_saved[0], 1)
            dve.wait_ge(turn_saved[0], 1)
            copy(vecs[:, :, DENSE], x_t[:, 0:P]).then_inc(x_placed, 1)

            def save_look_ups(t):
                dve.wait_ge(looked[0], t + 1)
                copy(vecs[:, :, 0:PER_BANK], spread(look_ps[:, 0, :], PER_BANK)).then_inc(look_saved[0], 1)

            save_look_ups(0)

            def tile(t, last):
                for u in range(0, len(RAW_GROUPS), 2):
                    dve.wait_ge(turned, t * USES + (2 + u + 1))
                    copy(vecs[:, :, slots_of(RAW_GROUPS[u])], spread(turn_ps[:, 0, :], len(RAW_GROUPS[u]))
                         ).then_inc(turn_saved[0], 1)
                dve.wait_ge(gram_done[0], t + 1)
                copy(gram[:, :, 0:QB], gram_ps[:, 0, 0:QB * SLOTS].rearrange("p (q g) -> p g q", g=SLOTS)
                     ).then_inc(gram_saved[0], 1)
                if not last:
                    dve.wait_ge(gram_done[1], t + 1)
                    dve.wait_ge(turn_saved[1], 1)
                    copy(vecs[:, :, DENSE], x_t[:, bass.ts(t + 1, P)]).then_inc(x_placed, 1)
                for u in range(len(RAW_GROUPS), USES):
                    if u % 2 == 0:
                        dve.wait_ge(turned, t * USES + (2 + u + 1))
                        pack(copy, t, u).then_inc(turn_saved[0], 1)
                dve.wait_ge(pairs_turned, t + 1)
                copy(pairs_t[:, :, 0:2 * JQ].rearrange("p c (j q) -> p j c q", j=2),
                     gram_ps[:, 0, 0:2 * PAIR_CHUNKS * JQ].rearrange("p (j c q) -> p j c q", j=2, c=PAIR_CHUNKS)
                     ).then_inc(pairs_saved[0], 1)
                if not last:
                    save_look_ups(t + 1)
                dve.wait_ge(h1_done, t + 1)
                for n in range(2):
                    ins = nc.vector.tensor_scalar(h1[:, n, :], mlp_ps[:, 0, n * P:(n + 1) * P], b1_sb[:, n:n + 1],
                                                  0.0, ALU.add, ALU.max)
                ins.then_inc(h1_saved[0], 1)
                dve.wait_ge(h2_done, t + 1)
                nc.vector.tensor_scalar(h2[:, 0, :], mlp_ps[:, 0, 2 * P:3 * P], b2_sb[:, 0:1], 0.0, ALU.add,
                                        ALU.max).then_inc(h2_saved[0], 1)
                dve.wait_ge(y_done, t + 1)
                copy(y[:, bass.ts(t, P)], mlp_ps[0:1, 0, 3 * P:4 * P]).then_inc(y_saved, 1)

            dve.wait_ge(small_landed, 48)
            with dve.Fori(0, TILES - 1) as t:
                tile(t, False)
            tile(TILES - 1, True)

        @block.scalar
        def _(act):
            copy = nc.scalar.copy
            act.dma_start(ids_wide[:].rearrange("p f b -> p (f b)"),
                          ids_onehot.rearrange("(o f) b -> o (f b)", o=1).to_broadcast([P, NO * BATCH])
                          ).then_inc(wide_landed, 16)
            for i in range(0, NO, 2):
                act.dma_start(table[0:ROWS, CHUNK0[i]:CHUNK0[i] + CHUNKS[i], :],
                              tables[ONEHOT_FIELDS[i]].rearrange("(p k) d -> p k d", p=ROWS)
                              ).then_inc(table_landed[i], 16)
            act.dma_start(w1_sb[:].rearrange("p c n -> p (c n)"), w1).then_inc(w1_landed, 16)
            act.dma_start(w2_sb[:], w2.rearrange("(n p) m -> p n m", p=P)).then_inc(w2_landed, 16)
            act.dma_start(b1_sb[:], b1).then_inc(small_landed, 16)
            act.dma_start(b2_sb[:], b2).then_inc(small_landed, 16)
            act.dma_start(w3_sb[:], w3).then_inc(small_landed, 16)
            act.wait_ge(turned, 2)
            copy(x_t[:, 2 * P:4 * P], turn_ps[:, 1, 0:2 * P]).then_inc(turn_saved[1], 1)

            def save_look_ups(t):
                act.wait_ge(looked[1], t + 1)
                copy(vecs[:, :, PER_BANK:NO], spread(look_ps[:, 1, :], NO - PER_BANK)).then_inc(look_saved[1], 1)

            save_look_ups(0)

            def tile(t, last):
                for u in range(1, len(RAW_GROUPS), 2):
                    act.wait_ge(turned, t * USES + (2 + u + 1))
                    copy(vecs[:, :, slots_of(RAW_GROUPS[u])], spread(turn_ps[:, 1, :], len(RAW_GROUPS[u]))
                         ).then_inc(turn_saved[1], 1)
                act.wait_ge(gram_done[1], t + 1)
                copy(gram[:, :, QB:JQ], gram_ps[:, 1, 0:QB * SLOTS].rearrange("p (q g) -> p g q", g=SLOTS)
                     ).then_inc(gram_saved[1], 1)
                for u in range(len(RAW_GROUPS), USES):
                    if u % 2 == 1:
                        act.wait_ge(turned, t * USES + (2 + u + 1))
                        pack(copy, t, u).then_inc(turn_saved[1], 1)
                act.wait_ge(pairs_turned, t + 1)
                copy(pairs_t[:, :, 2 * JQ:].rearrange("p c (j q) -> p j c q", j=2),
                     gram_ps[:, 1, 0:2 * PAIR_CHUNKS * JQ].rearrange("p (j c q) -> p j c q", j=2, c=PAIR_CHUNKS)
                     ).then_inc(pairs_saved[1], 1)
                act.wait_ge(h1_done, t + 1)
                for n in range(2, N1):
                    ins = nc.scalar.activation(h1[:, n, :], mlp_ps[:, 1, (n - 2) * P:(n - 1) * P], ACT.Relu,
                                               bias=b1_sb[:, n:n + 1])
                ins.then_inc(h1_saved[1], 1)
                act.wait_ge(h2_done, t + 1)
                nc.scalar.activation(h2[:, 1, :], mlp_ps[:, 1, 2 * P:3 * P], ACT.Relu,
                                     bias=b2_sb[:, 1:2]).then_inc(h2_saved[1], 1)
                if not last:
                    save_look_ups(t + 1)

            act.wait_ge(small_landed, 48)
            with act.Fori(0, TILES - 1) as t:
                tile(t, False)
            tile(TILES - 1, True)


def kernel(**inputs):
    import numpy as np
    import concourse.bacc as bacc
    from concourse.bass_utils import run_bass_kernel_spmd

    row_of = {}
    for i in range(SLOTS):
        for j in range(i + 1, SLOTS):
            row_of[i, j] = len(row_of)
    order = [row_of[tuple(sorted((SLOT_FIELDS[f], SLOT_FIELDS[g])))] for g in range(1, SLOTS) for f in range(g)]
    w1_in = np.asarray(inputs["W_top1"])
    w1 = np.zeros(((PAIR_CHUNKS + 1) * P, H1), w1_in.dtype)
    w1[:PAIRS] = w1_in[np.array(order)]
    w1[PAIR_CHUNKS * P:] = w1_in[PAIRS:]
    ids = np.asarray(inputs["ids"])

    arrays = {
        "ids_gather": ids[:, GATHER_FIELDS],
        "ids_onehot": ids[:, ONEHOT_FIELDS].T,
        "x": inputs["r_dense_x"],
        "w1": w1.reshape(PAIR_CHUNKS + 1, P, H1).transpose(1, 0, 2).reshape(P, -1),
        "b1": np.asarray(inputs["b_top1"]).reshape(N1, P).T,
        "w2": inputs["W_top2"],
        "b2": np.asarray(inputs["b_top2"]).reshape(N2, P).T,
        "w3": np.asarray(inputs["W_top3"]).reshape(N2, P).T,
    }
    for f in range(FIELDS):
        arrays[f"tbl_{f}"] = inputs[f"tbl_{f}"]
    nc = bacc.Bacc("TRN2", target_bir_lowering=False, num_devices=1)
    given, dram = {}, {}
    for name, a in arrays.items():
        given[f"{name}_dram"] = np.ascontiguousarray(a)
        dram[name] = nc.dram_tensor(f"{name}_dram", given[f"{name}_dram"].shape,
                                    mybir.dt.from_np(given[f"{name}_dram"].dtype), kind="ExternalInput").ap()
    out = nc.dram_tensor("out_dram", (BATCH, 1), F32, kind="ExternalOutput").ap()
    build(nc, dram["ids_gather"], dram["ids_onehot"], dram["x"], [dram[f"tbl_{f}"] for f in range(FIELDS)],
          dram["w1"], dram["b1"], dram["w2"], dram["b2"], dram["w3"], out)
    result = run_bass_kernel_spmd(nc, [given], core_ids=[0])
    return result.results[0]["out_dram"]
```

```python
from contextlib import ExitStack

import concourse.bass as bass
from concourse import mybir

F32 = mybir.dt.float32
F32R = mybir.dt.float32r
I32 = mybir.dt.int32
ALU = mybir.AluOpType
ACT = mybir.ActivationFunctionType

P = 128
TILES = 4
BATCH = TILES * P
FIELDS = 26
SLOTS = FIELDS + 1
D = 128
VOCAB = [1250, 12500, 1250, 1000, 1250, 1250, 125000, 12500, 1250, 1000, 1000, 1250, 1000,
         12500, 12500, 12500, 12500, 1250, 12500, 12500, 1250, 1250, 1000, 1250, 1250, 1000]

EARLY_FIELDS = [3, 9, 10, 12, 22]
LATE_FIELDS = [25, 0, 2, 4]
ONEHOT_FIELDS = EARLY_FIELDS + LATE_FIELDS
GATHER_FIELDS = [f for f in range(FIELDS) if f not in ONEHOT_FIELDS]
SLOT_FIELDS = EARLY_FIELDS + [FIELDS] + LATE_FIELDS + GATHER_FIELDS
NE = len(EARLY_FIELDS)
NL = len(LATE_FIELDS)
NO = len(ONEHOT_FIELDS)
NG = len(GATHER_FIELDS)
DENSE = NE
KNOWN = NO + 1

ROWS = 125
CHUNKS = [VOCAB[f] // ROWS for f in ONEHOT_FIELDS]
CHUNK0 = [sum(CHUNKS[:i]) for i in range(NO)]
MAX_CHUNKS = max(CHUNKS)
HIGHS = 4

GROUP_SIZES = [4, 4, 4, 3, 2]
GROUPS = [range(sum(GROUP_SIZES[:i]), sum(GROUP_SIZES[:i + 1])) for i in range(len(GROUP_SIZES))]
NGROUPS = len(GROUPS)
HALF_GROUPS = [range(2), range(2, NGROUPS)]
HALVES = [slice(0, GROUPS[1].stop), slice(GROUPS[1].stop, NG)]
JQ = P // 4
QB = JQ // 2
H1 = 512
H2 = 256
N1 = H1 // P
N2 = H2 // P

PACKS = [
    (1, 0, [(2, 2, 13)]),
    (2, 0, [(4, 4, 6), (1, 0, 2), (0, 1, 2)]),
    (26, 24, [(0, 1, 2)]),
    (4, 0, [(8, 8, 3), (1, 0, 4), (0, 1, 4)]),
    (8, 0, [(1, 0, 8), (0, 1, 8)]),
    (24, 16, [(1, 0, 3), (0, 1, 8)]),
    (16, 0, [(1, 0, 11), (0, 1, 16)]),
]


def pack_order():
    order = []
    for g0, f0, dims in PACKS:
        box = [(f0, g0)]
        for step_g, step_f, count in dims:
            box = [(f + n * step_f, g + n * step_g) for f, g in box for n in range(count)]
        order += box
    return order


PAIRS = SLOTS * (SLOTS - 1) // 2
assert sorted(pack_order()) == [(f, g) for f in range(SLOTS) for g in range(f + 1, SLOTS)]
PAIR_CHUNKS = -(-PAIRS // P)

LATE_AFTER = {"gram": [NE], "pairs": [NE + 1], "layer1": [NE + 2], "layer2": [NE + 3]}
EARLY_GROUPS = 2
TURN_AFTER = {NE - 4: "late", NE - 3: 0, NE - 2: 1}


def slot(i):
    return i if i < NE else i + 1


def build(nc, ids_gather, ids_late_in, ids_onehot, x, tables, w1, b1, w2, b2, w3, out):
    with ExitStack() as ctx:
        def sb(name, shape, dt=F32):
            return ctx.enter_context(nc.sbuf_tensor(name, shape, dt))

        def sem(name):
            return ctx.enter_context(nc.semaphore(name))

        ident = sb("ident", [P, P])
        zeros = sb("zeros", [P, P])
        row_ids = sb("row_ids", [P, 2, MAX_CHUNKS])
        ids_now = sb("ids_now", [P, NG], I32)
        ids_late = sb("ids_late", [P, NL], I32)
        ids_wide = sb("ids_wide", [P, NO, BATCH], I32)
        table = sb("table", [P, sum(CHUNKS), D])
        high = sb("high", [P, HIGHS, MAX_CHUNKS, D], F32R)
        low = sb("low", [P, 2, MAX_CHUNKS, D], F32R)
        onehot = sb("onehot", [P, 2, MAX_CHUNKS, BATCH], F32R)
        rows = sb("rows", [P, NG, D])
        rows_late = sb("rows_late", [P, NL, D])
        x_rows = sb("x_rows", [P, TILES, D])
        known = sb("known", [P, KNOWN, BATCH])
        vecs = sb("vecs", [P, P, SLOTS])
        dots = sb("dots", [P, SLOTS, 32])
        pairs = sb("pairs", [P, PAIR_CHUNKS * P])
        pairs_t = sb("pairs_t", [P, PAIR_CHUNKS, P])
        w1_sb = sb("w1_sb", [P, PAIR_CHUNKS + 1, H1])
        w2_sb = sb("w2_sb", [P, N1, H2])
        w3_sb = sb("w3_sb", [P, N2])
        b1_sb = sb("b1_sb", [P, N1])
        b2_sb = sb("b2_sb", [P, N2])
        h1 = sb("h1", [P, N1, P])
        h2 = sb("h2", [P, N2, P])
        y = sb("y", [1, BATCH])

        turn_ps = ctx.enter_context(nc.psum_tensor("turn_ps", [P, 2, 512], F32))
        look_ps = ctx.enter_context(nc.psum_tensor("look_ps", [P, 2, 512], F32))
        gram_ps = ctx.enter_context(nc.psum_tensor("gram_ps", [P, 2, 512], F32))
        mlp_ps = ctx.enter_context(nc.psum_tensor("mlp_ps", [P, 2, 512], F32))

        ids_landed = [sem("ids_landed_a"), sem("ids_landed_b")]
        ids_late_landed = sem("ids_late_landed")
        wide_landed = [sem(f"wide_landed{i}") for i in range(NO)]
        x_landed = sem("x_landed")
        table_landed = [sem(f"table_landed{i}") for i in range(NO)]
        w1_landed, w2_landed, small_landed = sem("w1_landed"), sem("w2_landed"), sem("small_landed")
        rows_landed = [sem(f"rows_landed{g}") for g in range(NGROUPS)]
        rows_late_landed = sem("rows_late_landed")
        group_begun = sem("group_begun")
        blank = sem("blank")
        consts_ready = sem("consts_ready")
        zeros_ready = sem("zeros_ready")
        high_ready = sem("high_ready")
        low_ready = sem("low_ready")
        onehot_ready = sem("onehot_ready")
        turned = sem("turned")
        turn_saved = sem("turn_saved")
        looked = sem("looked")
        look_saved = sem("look_saved")
        known_placed = sem("known_placed")
        gram_done = sem("gram_done")
        dots_ready = sem("dots_ready")
        pairs_packed = sem("pairs_packed")
        pairs_turned = sem("pairs_turned")
        pairs_saved = [sem("pairs_saved_dve"), sem("pairs_saved_act")]
        h1_done = sem("h1_done")
        h1_saved = [sem("h1_saved_dve"), sem("h1_saved_act")]
        h2_done = sem("h2_done")
        h2_saved = [sem("h2_saved_dve"), sem("h2_saved_act")]
        y_done = sem("y_done")
        y_saved = sem("y_saved")
        out_landed = sem("out_landed")

        ids_tiles = ids_gather.rearrange("(t p) f -> t p f", p=P)
        h_cols = [slice(n * P, (n + 1) * P) for n in range(4)]

        def samples(i):
            return slice(0 if i < NE else P, BATCH)

        def table_of(i):
            return table[0:ROWS, CHUNK0[i]:CHUNK0[i] + CHUNKS[i], :]

        def high_of(i):
            return high[0:ROWS, i % HIGHS, 0:CHUNKS[i], :]

        def low_of(i):
            return low[0:ROWS, i % 2, 0:CHUNKS[i], :]

        def table_dma(eng, i):
            eng.dma_start(table[0:ROWS, CHUNK0[i]:CHUNK0[i] + CHUNKS[i], :],
                          tables[ONEHOT_FIELDS[i]].rearrange("(p k) d -> p k d", p=ROWS)
                          ).then_inc(table_landed[i], 16)

        def wide_dma(eng, i):
            eng.dma_start(ids_wide[:, i, :], ids_onehot[i * BATCH:(i + 1) * BATCH].rearrange("(o n) -> o n", o=1)
                          .to_broadcast([P, BATCH])).then_inc(wide_landed[i], 16)

        block = ctx.enter_context(nc.Block())

        @block.sync
        def _(sp):
            sp.dma_start(ids_late[:], ids_late_in).then_inc(ids_late_landed, 16)
            for h in range(2):
                sp.dma_start(ids_now[:, HALVES[h]], ids_tiles[0, :, HALVES[h]]).then_inc(ids_landed[h], 16)
            for i in range(NO):
                table_dma(sp, i)
            sp.dma_start(w1_sb[:].rearrange("p c n -> p (c n)"), w1).then_inc(w1_landed, 16)
            sp.dma_start(w2_sb[:], w2.rearrange("(n p) m -> p n m", p=P)).then_inc(w2_landed, 16)
            with sp.Fori(0, TILES - 1) as t:
                for h in range(2):
                    for g in HALF_GROUPS[h]:
                        sp.wait_ge(rows_landed[g], t * (16 * len(GROUPS[g])) + 16 * len(GROUPS[g]))
                    sp.dma_start(ids_now[:, HALVES[h]], ids_tiles[t + 1, :, HALVES[h]]
                                 ).then_inc(ids_landed[h], 16)
            sp.wait_ge(y_saved, TILES)
            sp.dma_start(out.rearrange("b o -> o b"), y[:]).then_inc(out_landed, 16)
            sp.wait_ge(out_landed, 16)

        @block.gpsimd
        def _(pool):
            nc.gpsimd.memset(ident[:], 0.0).then_inc(blank, 1)
            pool.wait_ge(blank, 1)
            nc.gpsimd.affine_select(out=ident[:], in_=ident[:], compare_op=ALU.not_equal, fill=1.0, base=0,
                                    pattern=[[-1, P]], channel_multiplier=1).then_inc(consts_ready, 1)
            for i, n in enumerate((8, 10)):
                nc.gpsimd.iota(row_ids[:, i, 0:n], pattern=[[1, n]], base=0, channel_multiplier=n,
                               allow_small_or_imprecise_dtypes=True).then_inc(consts_ready, 1)

            def gather_tile(t, first):
                for h in range(2):
                    pool.wait_ge(ids_landed[h], t * 16 + 16)
                    for g in HALF_GROUPS[h]:
                        if not first:
                            pool.wait_ge(turned, t * NGROUPS + (g + 3 - NGROUPS))
                            pool.sem_inc(group_begun, 1)
                        for i in GROUPS[g]:
                            nc.gpsimd.indirect_dma_start(
                                rows[:, i, :], None, tables[GATHER_FIELDS[i]],
                                bass.IndirectOffsetOnAxis(ap=ids_now[:, i:i + 1], axis=0)
                            ).then_inc(rows_landed[g], 16)

            pool.wait_ge(ids_late_landed, 16)
            for i in range(NL):
                nc.gpsimd.indirect_dma_start(
                    rows_late[:, i, :], None, tables[LATE_FIELDS[i]],
                    bass.IndirectOffsetOnAxis(ap=ids_late[:, i:i + 1], axis=0)).then_inc(rows_late_landed, 16)
            gather_tile(0, True)
            with pool.Fori(1, TILES) as t:
                gather_tile(t, False)

        @block.tensor
        def _(pe):
            def look_up(i):
                if i >= 2:
                    pe.wait_ge(look_saved, i - 1)
                pe.wait_ge(onehot_ready, i + 1)
                pe.wait_ge(low_ready, i + 1)
                products = [(part[:, k, :], k) for k in range(CHUNKS[i]) for part in (high_of(i), low_of(i))]
                for n, (rows_of_table, k) in enumerate(products):
                    mm = nc.tensor.matmul(look_ps[:, i % 2, samples(i)], rows_of_table,
                                          onehot[0:ROWS, i % 2, k, samples(i)],
                                          start=(n == 0), stop=(n == len(products) - 1))
                mm.then_inc(looked, 1)

            def turn_group(t, u):
                pe.wait_ge(turn_saved, t * NGROUPS + (u + 1))
                pe.wait_ge(rows_landed[u], t * (16 * len(GROUPS[u])) + 16 * len(GROUPS[u]))
                for n, i in enumerate(GROUPS[u]):
                    mm = nc.tensor.transpose(turn_ps[:, u % 2, n * P:(n + 1) * P], rows[:, i, :], ident[:])
                mm.then_inc(turned, 1)

            pe.wait_ge(zeros_ready, 1)
            for b in range(2):
                for q in range(0, QB, 4):
                    nc.tensor.matmul(gram_ps[:, b, q * SLOTS:(q + 4) * SLOTS], zeros[:], zeros[:, 0:4 * SLOTS],
                                     start=True, stop=True)
            pe.wait_ge(consts_ready, 3)
            pe.wait_ge(x_landed, 16)
            for i in range(TILES):
                mm = nc.tensor.transpose(turn_ps[:, 0, i * P:(i + 1) * P], x_rows[:, i, :], ident[:])
            mm.then_inc(turned, 1)
            for i in range(NE):
                look_up(i)
                if TURN_AFTER.get(i) == "late":
                    pe.wait_ge(rows_late_landed, 16 * NL)
                    for n in range(NL):
                        mm = nc.tensor.transpose(turn_ps[:, 1, n * P:(n + 1) * P], rows_late[:, n, :], ident[:])
                    mm.then_inc(turned, 1)
                elif i in TURN_AFTER:
                    turn_group(0, TURN_AFTER[i])

            def late_look_ups(step):
                for i in LATE_AFTER.get(step, []):
                    look_up(i)

            def tile(t, first, last):
                for u in range(EARLY_GROUPS if first else 0, NGROUPS):
                    turn_group(t, u)
                pe.wait_ge(known_placed, t + 1)
                pe.wait_ge(turn_saved, t * NGROUPS + NGROUPS + 2)
                for b in range(2):
                    for q in range(QB):
                        for j in range(4):
                            v = vecs[:, j * JQ + b * QB + q, :]
                            mm = nc.tensor.matmul(gram_ps[32 * j:32 * j + SLOTS, b, q * SLOTS:(q + 1) * SLOTS],
                                                  v, v, start=True, stop=True)
                mm.then_inc(gram_done, 1)
                for n in range(N1):
                    nc.tensor.matmul(mlp_ps[:, n // 2, h_cols[n % 2]], w1_sb[:, PAIR_CHUNKS, n * P:(n + 1) * P],
                                     known[:, DENSE, bass.ts(t, P)], start=(n % 2 == 0), stop=False, skip_group_check=True)
                if first:
                    late_look_ups("gram")
                pe.wait_ge(pairs_packed, t + 1)
                for c in range(PAIR_CHUNKS):
                    mm = nc.tensor.transpose(gram_ps[:, c // 2, (c % 2) * P:(c % 2 + 1) * P],
                                             pairs[:, c * P:(c + 1) * P], ident[:])
                mm.then_inc(pairs_turned, 1)
                if first:
                    late_look_ups("pairs")
                for b in range(2):
                    pe.wait_ge(pairs_saved[b], t + 1)
                for n in range(N1):
                    for c in range(PAIR_CHUNKS):
                        mm = nc.tensor.matmul(mlp_ps[:, n // 2, h_cols[n % 2]], w1_sb[:, c, n * P:(n + 1) * P],
                                              pairs_t[:, c, :], start=False, stop=(c == PAIR_CHUNKS - 1),
                                              skip_group_check=True)
                mm.then_inc(h1_done, 1)
                if first:
                    late_look_ups("layer1")
                for b in range(2):
                    pe.wait_ge(h1_saved[b], t + 1)
                for m in range(N2):
                    for n in range(N1):
                        mm = nc.tensor.matmul(mlp_ps[:, m, h_cols[2]], w2_sb[:, n, m * P:(m + 1) * P],
                                              h1[:, n, :], start=(n == 0), stop=(n == N1 - 1))
                mm.then_inc(h2_done, 1)
                if first:
                    late_look_ups("layer2")
                for b in range(2):
                    pe.wait_ge(h2_saved[b], t + 1)
                for m in range(N2):
                    mm = nc.tensor.matmul(mlp_ps[0:1, 1, h_cols[3]], w3_sb[:, m:m + 1], h2[:, m, :],
                                          start=(m == 0), stop=(m == N2 - 1))
                mm.then_inc(y_done, 1)
                if not last:
                    pe.wait_ge(y_saved, t + 1)

            pe.wait_ge(w1_landed, 16)
            pe.wait_ge(w2_landed, 16)
            pe.wait_ge(small_landed, 48)
            tile(0, True, False)
            with pe.Fori(1, TILES - 1) as t:
                tile(t, False, False)
            tile(TILES - 1, False, True)

        @block.vector
        def _(dve):
            copy = nc.vector.tensor_copy

            def make_look_up(i):
                dve.wait_ge(wide_landed[i], 16)
                if i >= 2:
                    dve.wait_ge(looked, i - 1)
                for k in range(CHUNKS[i]):
                    ins = nc.vector.tensor_scalar(onehot[:, i % 2, k, samples(i)], ids_wide[:, i, samples(i)],
                                                  row_ids[:, (CHUNKS[i] - 8) // 2, k:k + 1], None, ALU.is_equal)
                ins.then_inc(onehot_ready, 1)
                dve.wait_ge(high_ready, i + 1)
                nc.vector.tensor_tensor(low_of(i), table_of(i), high_of(i).bitcast(F32), ALU.subtract
                                        ).then_inc(low_ready, 1)

            def late_look_ups(step):
                for i in LATE_AFTER[step]:
                    make_look_up(i)

            nc.vector.memset(zeros[:], 0.0).then_inc(zeros_ready, 1)
            nc.vector.memset(pairs[:, PAIRS:], 0.0)
            dve.wait_ge(consts_ready, 3)
            for i in range(NE):
                make_look_up(i)

            def tile(t, first, last):
                if first:
                    late_look_ups("gram")
                dve.wait_ge(gram_done, t + 1)
                nc.vector.transpose(dots[:], gram_ps[:, :, 0:QB * SLOTS].rearrange("p h (q g) -> p g h q", g=SLOTS)
                                    ).then_inc(dots_ready, 1)
                dve.wait_ge(dots_ready, t + 1)
                at = 0
                for g, f, dims in PACKS:
                    n = 1
                    for _, _, count in dims:
                        n *= count
                    src = bass.AP(tensor=dots[:].tensor, offset=g * 32 + f,
                                  ap=[[SLOTS * 32, P]] + [[32 * step_g + step_f, count]
                                                          for step_g, step_f, count in dims])
                    names = "abc"[:len(dims)]
                    dst = pairs[:, at:at + n]
                    if len(dims) > 1:
                        dst = dst.rearrange(f"p ({' '.join(names)}) -> p {' '.join(names)}",
                                            **{x: d[2] for x, d in zip(names, dims)})
                    ins = copy(dst, src)
                    at += n
                ins.then_inc(pairs_packed, 1)
                if first:
                    late_look_ups("pairs")
                dve.wait_ge(pairs_turned, t + 1)
                copy(pairs_t[:, 0:2, :], gram_ps[:, 0, 0:2 * P].rearrange("p (c b) -> p c b", c=2)
                     ).then_inc(pairs_saved[0], 1)
                if first:
                    late_look_ups("layer1")
                dve.wait_ge(h1_done, t + 1)
                for n in range(2):
                    ins = nc.vector.tensor_scalar(h1[:, n, :], mlp_ps[:, 0, h_cols[n]], b1_sb[:, n:n + 1],
                                                  0.0, ALU.add, ALU.max)
                ins.then_inc(h1_saved[0], 1)
                if first:
                    late_look_ups("layer2")
                dve.wait_ge(h2_done, t + 1)
                nc.vector.tensor_scalar(h2[:, 0, :], mlp_ps[:, 0, h_cols[2]], b2_sb[:, 0:1], 0.0, ALU.add,
                                        ALU.max).then_inc(h2_saved[0], 1)

            dve.wait_ge(small_landed, 48)
            tile(0, True, False)
            with dve.Fori(1, TILES - 1) as t:
                tile(t, False, False)
            tile(TILES - 1, False, True)

        @block.scalar
        def _(act):
            copy = nc.scalar.copy
            act.dma_start(x_rows[:], x.rearrange("(t p) d -> p t d", p=P)).then_inc(x_landed, 16)
            for i in range(NO):
                wide_dma(act, i)
            act.dma_start(b1_sb[:], b1).then_inc(small_landed, 16)
            act.dma_start(b2_sb[:], b2).then_inc(small_landed, 16)
            act.dma_start(w3_sb[:], w3).then_inc(small_landed, 16)

            def spread(bank, n):
                return bank[:, 0:n * P].rearrange("p (s b) -> p b s", b=P)

            def make_high(i):
                act.wait_ge(table_landed[i], 16)
                if i >= HIGHS:
                    act.wait_ge(looked, i - HIGHS + 1)
                copy(high_of(i), table_of(i)).then_inc(high_ready, 1)

            def save_look_up(i):
                act.wait_ge(looked, i + 1)
                copy(known[:, slot(i), samples(i)], look_ps[:, i % 2, samples(i)]).then_inc(look_saved, 1)

            def save_late(step):
                for i in LATE_AFTER[step]:
                    save_look_up(i)

            def place(t, n):
                copy(vecs[:, :, 0:n], known[:, 0:n, bass.ts(t, P)].rearrange("p s b -> p b s")
                     ).then_inc(known_placed, 1)

            def save_group(t, u):
                act.wait_ge(turned, t * NGROUPS + (u + 3))
                copy(vecs[:, :, KNOWN + GROUPS[u].start:KNOWN + GROUPS[u].stop],
                     spread(turn_ps[:, u % 2, :], len(GROUPS[u]))).then_inc(turn_saved, 1)

            act.wait_ge(turned, 1)
            copy(known[:, DENSE, :], turn_ps[:, 0, :]).then_inc(turn_saved, 1)
            for i in range(2):
                make_high(i)
            for i in range(NE):
                if i + 2 < NO:
                    make_high(i + 2)
                save_look_up(i)
                if TURN_AFTER.get(i) == "late":
                    act.wait_ge(turned, 2)
                    copy(vecs[:, :, NE + 1:KNOWN], spread(turn_ps[:, 1, :], NL)).then_inc(turn_saved, 1)
                elif i in TURN_AFTER:
                    save_group(0, TURN_AFTER[i])
            act.wait_ge(turn_saved, 1)
            act.wait_ge(look_saved, NE)
            place(0, NE + 1)

            def tile(t, first, last):
                for u in range(EARLY_GROUPS if first else 0, NGROUPS):
                    save_group(t, u)
                if first:
                    for i in range(NE + 2, NO):
                        make_high(i)
                    save_late("gram")
                elif not last:
                    act.wait_ge(gram_done, t + 1)
                    place(t + 1, KNOWN)
                act.wait_ge(pairs_turned, t + 1)
                copy(pairs_t[:, 2, :], gram_ps[:, 1, 0:P]).then_inc(pairs_saved[1], 1)
                if first:
                    save_late("pairs")
                act.wait_ge(h1_done, t + 1)
                for n in range(2, N1):
                    ins = nc.scalar.activation(h1[:, n, :], mlp_ps[:, 1, h_cols[n - 2]], ACT.Relu,
                                               bias=b1_sb[:, n:n + 1])
                ins.then_inc(h1_saved[1], 1)
                if first:
                    save_late("layer1")
                act.wait_ge(h2_done, t + 1)
                nc.scalar.activation(h2[:, 1, :], mlp_ps[:, 1, h_cols[2]], ACT.Relu,
                                     bias=b2_sb[:, 1:2]).then_inc(h2_saved[1], 1)
                if first:
                    save_late("layer2")
                act.wait_ge(y_done, t + 1)
                copy(y[:, bass.ts(t, P)], mlp_ps[0:1, 1, h_cols[3]]).then_inc(y_saved, 1)
                if first:
                    act.wait_ge(gram_done, t + 1)
                    act.wait_ge(look_saved, NO)
                    place(t + 1, KNOWN)

            act.wait_ge(small_landed, 48)
            tile(0, True, False)
            with act.Fori(1, TILES - 1) as t:
                tile(t, False, False)
            tile(TILES - 1, False, True)


def kernel(**inputs):
    import numpy as np
    import concourse.bacc as bacc
    from concourse.bass_utils import run_bass_kernel_spmd

    row_of = {}
    for i in range(SLOTS):
        for j in range(i + 1, SLOTS):
            row_of[i, j] = len(row_of)
    order = [row_of[tuple(sorted((SLOT_FIELDS[f], SLOT_FIELDS[g])))] for f, g in pack_order()]
    w1_in = np.asarray(inputs["W_top1"])
    w1 = np.zeros(((PAIR_CHUNKS + 1) * P, H1), w1_in.dtype)
    w1[:PAIRS] = w1_in[np.array(order)]
    w1[PAIR_CHUNKS * P:] = w1_in[PAIRS:]
    ids = np.asarray(inputs["ids"])

    arrays = {
        "ids_gather": ids[:, GATHER_FIELDS],
        "ids_late": ids[:P, LATE_FIELDS],
        "ids_onehot": ids[:, ONEHOT_FIELDS].T.reshape(-1),
        "x": inputs["r_dense_x"],
        "w1": w1.reshape(PAIR_CHUNKS + 1, P, H1).transpose(1, 0, 2).reshape(P, -1),
        "b1": np.asarray(inputs["b_top1"]).reshape(N1, P).T,
        "w2": inputs["W_top2"],
        "b2": np.asarray(inputs["b_top2"]).reshape(N2, P).T,
        "w3": np.asarray(inputs["W_top3"]).reshape(N2, P).T,
    }
    for f in range(FIELDS):
        arrays[f"tbl_{f}"] = inputs[f"tbl_{f}"]
    nc = bacc.Bacc("TRN2", target_bir_lowering=False, num_devices=1)
    given, dram = {}, {}
    for name, a in arrays.items():
        given[f"{name}_dram"] = np.ascontiguousarray(a)
        dram[name] = nc.dram_tensor(f"{name}_dram", given[f"{name}_dram"].shape,
                                    mybir.dt.from_np(given[f"{name}_dram"].dtype), kind="ExternalInput").ap()
    out = nc.dram_tensor("out_dram", (BATCH, 1), F32, kind="ExternalOutput").ap()
    build(nc, dram["ids_gather"], dram["ids_late"], dram["ids_onehot"], dram["x"], [dram[f"tbl_{f}"] for f in range(FIELDS)],
          dram["w1"], dram["b1"], dram["w2"], dram["b2"], dram["w3"], out)
    result = run_bass_kernel_spmd(nc, [given], core_ids=[0])
    return result.results[0]["out_dram"]
```

```python
from contextlib import ExitStack

import concourse.bass as bass
from concourse import mybir

F32 = mybir.dt.float32
F32R = mybir.dt.float32r
I32 = mybir.dt.int32
ALU = mybir.AluOpType
ACT = mybir.ActivationFunctionType

P = 128
TILES = 4
BATCH = TILES * P
FIELDS = 26
SLOTS = FIELDS + 1
D = 128
VOCAB = [1250, 12500, 1250, 1000, 1250, 1250, 125000, 12500, 1250, 1000, 1000, 1250, 1000,
         12500, 12500, 12500, 12500, 1250, 12500, 12500, 1250, 1250, 1000, 1250, 1250, 1000]

EARLY_FIELDS = [3, 9, 10, 12, 22]
LATE_FIELDS = [25, 0, 2, 4]
ONEHOT_FIELDS = EARLY_FIELDS + LATE_FIELDS
GATHER_FIELDS = [f for f in range(FIELDS) if f not in ONEHOT_FIELDS]
SLOT_FIELDS = EARLY_FIELDS + [FIELDS] + LATE_FIELDS + GATHER_FIELDS
NE = len(EARLY_FIELDS)
NL = len(LATE_FIELDS)
NO = len(ONEHOT_FIELDS)
NG = len(GATHER_FIELDS)
DENSE = NE
KNOWN = NO + 1

ROWS = 125
CHUNKS = [VOCAB[f] // ROWS for f in ONEHOT_FIELDS]
CHUNK0 = [sum(CHUNKS[:i]) for i in range(NO)]
MAX_CHUNKS = max(CHUNKS)
HELD = 4
MADE = 3

GROUP_SIZES = [4, 4, 4, 3, 2]
GROUPS = [range(sum(GROUP_SIZES[:i]), sum(GROUP_SIZES[:i + 1])) for i in range(len(GROUP_SIZES))]
NGROUPS = len(GROUPS)
HALF_GROUPS = [range(2), range(2, NGROUPS)]
HALVES = [slice(0, GROUPS[1].stop), slice(GROUPS[1].stop, NG)]
JQ = P // 4
QB = JQ // 2
H1 = 512
H2 = 256
N1 = H1 // P
N2 = H2 // P
N1_DVE = N1 - 1

PACKS = [
    (1, 0, [(2, 2, 13)]),
    (2, 0, [(4, 4, 6), (1, 0, 2), (0, 1, 2)]),
    (26, 24, [(0, 1, 2)]),
    (4, 0, [(8, 8, 3), (1, 0, 4), (0, 1, 4)]),
    (8, 0, [(1, 0, 8), (0, 1, 8)]),
    (24, 16, [(1, 0, 3), (0, 1, 8)]),
    (16, 0, [(1, 0, 11), (0, 1, 16)]),
]


def pack_order():
    order = []
    for g0, f0, dims in PACKS:
        box = [(f0, g0)]
        for step_g, step_f, count in dims:
            box = [(f + n * step_f, g + n * step_g) for f, g in box for n in range(count)]
        order += box
    return order


PAIRS = SLOTS * (SLOTS - 1) // 2
assert sorted(pack_order()) == [(f, g) for f in range(SLOTS) for g in range(f + 1, SLOTS)]
PAIR_CHUNKS = -(-PAIRS // P)

LATE_AFTER = {"gram": [NE], "pairs": [NE + 1], "layer1": [NE + 2, NE + 3]}
MAKE_BEFORE = {"dots": [NE, NE + 1], "pairs_t": [NE + 2], "h1": [NE + 3]}
TURN_AFTER = {1: ["late"], 2: [0, 1], 3: [2], 4: [3, 4]}
WX_AFTER, W1_AFTER, W2_AFTER = HELD, NE + 1, NE + 3
RELOAD_AFTER = {NE + 1: 0, NE + 2: 1}
START_GROUPS = [4]
NEXT_AFTER = {"gram": [0], "pairs": [1], "layer1": [2, 3]}
KEEP_CLOCK = 4


def slot(i):
    return i if i < NE else i + 1


def build(nc, ids_gather, ids_late_in, ids_onehot, x, tables, w1, b1, w2, b2, w3, out):
    with ExitStack() as ctx:
        def sb(name, shape, dt=F32):
            return ctx.enter_context(nc.sbuf_tensor(name, shape, dt))

        def sem(name):
            return ctx.enter_context(nc.semaphore(name))

        ident = sb("ident", [P, P])
        zeros = sb("zeros", [P, P])
        row_ids = sb("row_ids", [P, 2, MAX_CHUNKS])
        ids_now = sb("ids_now", [P, NG], I32)
        ids_late = sb("ids_late", [P, NL], I32)
        ids_wide = sb("ids_wide", [P, HELD, BATCH], I32)
        table = sb("table", [P, HELD, MAX_CHUNKS, D])
        high = sb("high", [P, HELD, MAX_CHUNKS, D], F32R)
        low = sb("low", [P, MADE, MAX_CHUNKS, D], F32R)
        onehot = sb("onehot", [P, MADE, MAX_CHUNKS, BATCH], F32R)
        rows = sb("rows", [P, NG, D])
        rows_late = sb("rows_late", [P, NL, D])
        x_rows = sb("x_rows", [P, TILES, D])
        known = sb("known", [P, KNOWN, BATCH])
        vecs = sb("vecs", [P, P, SLOTS])
        dots = sb("dots", [P, SLOTS, 32])
        pairs = sb("pairs", [P, PAIR_CHUNKS * P])
        pairs_t = sb("pairs_t", [P, PAIR_CHUNKS, P])
        w1_sb = sb("w1_sb", [P, PAIR_CHUNKS + 1, H1])
        w2_sb = sb("w2_sb", [P, N1, H2])
        w3_sb = sb("w3_sb", [P, N2])
        b1_sb = sb("b1_sb", [P, N1])
        b2_sb = sb("b2_sb", [P, N2])
        h1 = sb("h1", [P, N1, P])
        h2 = sb("h2", [P, N2, P])
        y = sb("y", [1, BATCH])

        turn_ps = ctx.enter_context(nc.psum_tensor("turn_ps", [P, 2, 512], F32))
        look_ps = ctx.enter_context(nc.psum_tensor("look_ps", [P, 2, 512], F32))
        gram_ps = ctx.enter_context(nc.psum_tensor("gram_ps", [P, 2, 512], F32))
        mlp_ps = ctx.enter_context(nc.psum_tensor("mlp_ps", [P, 2, 512], F32))

        ids_landed = [sem("ids_landed_a"), sem("ids_landed_b")]
        ids_late_landed = sem("ids_late_landed")
        wide_landed = [sem(f"wide_landed{i}") for i in range(NO)]
        x_landed = sem("x_landed")
        table_landed = [sem(f"table_landed{i}") for i in range(NO)]
        wx_landed, w1_landed, w2_landed, small_landed = sem("wx_landed"), sem("w1_landed"), sem("w2_landed"), sem("small_landed")
        rows_landed = [sem(f"rows_landed{g}") for g in range(NGROUPS)]
        rows_late_landed = sem("rows_late_landed")
        group_begun = sem("group_begun")
        blank = sem("blank")
        consts_ready = sem("consts_ready")
        zeros_ready = sem("zeros_ready")
        high_ready = sem("high_ready")
        low_ready = sem("low_ready")
        onehot_ready = sem("onehot_ready")
        turned = sem("turned")
        turn_saved = sem("turn_saved")
        looked = sem("looked")
        look_saved = sem("look_saved")
        known_placed = sem("known_placed")
        gram_done = sem("gram_done")
        dots_ready = sem("dots_ready")
        pairs_packed = sem("pairs_packed")
        pairs_turned = sem("pairs_turned")
        pairs_saved = [sem("pairs_saved_dve"), sem("pairs_saved_act")]
        h1_done = sem("h1_done")
        h1_saved = [sem("h1_saved_dve"), sem("h1_saved_act")]
        h2_done = sem("h2_done")
        h2_saved = [sem("h2_saved_dve"), sem("h2_saved_act")]
        y_done = sem("y_done")
        y_saved = sem("y_saved")
        out_landed = sem("out_landed")

        ids_tiles = ids_gather.rearrange("(t p) f -> t p f", p=P)
        h_cols = [slice(n * P, (n + 1) * P) for n in range(N1_DVE)]

        def samples(i):
            return slice(0 if i < NE else P, BATCH)

        def table_of(i):
            return table[0:ROWS, i % HELD, 0:CHUNKS[i], :]

        def high_of(i):
            return high[0:ROWS, i % HELD, 0:CHUNKS[i], :]

        def low_of(i):
            return low[0:ROWS, i % MADE, 0:CHUNKS[i], :]

        def table_dma(eng, i):
            eng.dma_start(table_of(i), tables[ONEHOT_FIELDS[i]].rearrange("(p k) d -> p k d", p=ROWS)
                          ).then_inc(table_landed[i], 16)

        def wide_dma(eng, i):
            eng.dma_start(ids_wide[:, i % HELD, :],
                          ids_onehot[i * BATCH:(i + 1) * BATCH].rearrange("(o n) -> o n", o=1)
                          .to_broadcast([P, BATCH])).then_inc(wide_landed[i], 16)

        block = ctx.enter_context(nc.Block())

        @block.sync
        def _(sp):
            def reload_ids(t, h):
                for g in HALF_GROUPS[h]:
                    sp.wait_ge(rows_landed[g], t * (16 * len(GROUPS[g])) + 16 * len(GROUPS[g]))
                sp.dma_start(ids_now[:, HALVES[h]], ids_tiles[t + 1, :, HALVES[h]]).then_inc(ids_landed[h], 16)

            sp.dma_start(ids_late[:], ids_late_in).then_inc(ids_late_landed, 16)
            table_dma(sp, 0)
            for h in range(2):
                sp.dma_start(ids_now[:, HALVES[h]], ids_tiles[0, :, HALVES[h]]).then_inc(ids_landed[h], 16)
            for i in range(1, HELD):
                wide_dma(sp, i)
                table_dma(sp, i)
            sp.dma_start(b1_sb[:], b1).then_inc(small_landed, 16)
            sp.dma_start(b2_sb[:], b2).then_inc(small_landed, 16)
            sp.dma_start(w3_sb[:], w3).then_inc(small_landed, 16)
            for i in range(HELD, NO):
                sp.wait_ge(onehot_ready, CHUNK0[i - HELD + 1])
                wide_dma(sp, i)
                sp.wait_ge(low_ready, i - HELD + 1)
                table_dma(sp, i)
                if i in RELOAD_AFTER:
                    reload_ids(0, RELOAD_AFTER[i])
                if i == WX_AFTER:
                    sp.dma_start(w1_sb[:, PAIR_CHUNKS, :], w1[:, PAIR_CHUNKS * H1:]).then_inc(wx_landed, 16)
                if i == W1_AFTER:
                    sp.dma_start(w1_sb[:, 0:PAIR_CHUNKS, :].rearrange("p c n -> p (c n)"), w1[:, 0:PAIR_CHUNKS * H1]
                                 ).then_inc(w1_landed, 16)
                if i == W2_AFTER:
                    sp.dma_start(w2_sb[:], w2.rearrange("(n p) m -> p n m", p=P)).then_inc(w2_landed, 16)
            with sp.Fori(1, TILES - 1) as t:
                for h in range(2):
                    reload_ids(t, h)
            sp.wait_ge(y_saved, TILES)
            sp.dma_start(out.rearrange("b o -> o b"), y[:]).then_inc(out_landed, 16)
            sp.wait_ge(out_landed, 16)

        @block.gpsimd
        def _(pool):
            nc.gpsimd.memset(ident[:], 0.0).then_inc(blank, 1)
            pool.wait_ge(blank, 1)
            nc.gpsimd.affine_select(out=ident[:], in_=ident[:], compare_op=ALU.not_equal, fill=1.0, base=0,
                                    pattern=[[-1, P]], channel_multiplier=1).then_inc(consts_ready, 1)
            for i, n in enumerate((8, 10)):
                nc.gpsimd.iota(row_ids[:, i, 0:n], pattern=[[1, n]], base=0, channel_multiplier=n,
                               allow_small_or_imprecise_dtypes=True).then_inc(consts_ready, 1)

            def gather_tile(t, first):
                for h in range(2):
                    pool.wait_ge(ids_landed[h], t * 16 + 16)
                    for g in HALF_GROUPS[h]:
                        if not first:
                            pool.wait_ge(turned, t * NGROUPS + (g + 3 - NGROUPS))
                            pool.sem_inc(group_begun, 1)
                        for i in GROUPS[g]:
                            nc.gpsimd.indirect_dma_start(
                                rows[:, i, :], None, tables[GATHER_FIELDS[i]],
                                bass.IndirectOffsetOnAxis(ap=ids_now[:, i:i + 1], axis=0)
                            ).then_inc(rows_landed[g], 16)

            pool.wait_ge(ids_late_landed, 16)
            for i in range(NL):
                nc.gpsimd.indirect_dma_start(
                    rows_late[:, i, :], None, tables[LATE_FIELDS[i]],
                    bass.IndirectOffsetOnAxis(ap=ids_late[:, i:i + 1], axis=0)).then_inc(rows_late_landed, 16)
            gather_tile(0, True)
            with pool.Fori(1, TILES) as t:
                gather_tile(t, False)

        @block.tensor
        def _(pe):
            def look_up(i):
                if i >= 2:
                    pe.wait_ge(look_saved, i - 1)
                pe.wait_ge(high_ready, i + 1)
                products = [(part[:, k, :], k) for part in (high_of(i), low_of(i)) for k in range(CHUNKS[i])]
                for n, (rows_of_table, k) in enumerate(products):
                    if n < CHUNKS[i]:
                        pe.wait_ge(onehot_ready, CHUNK0[i] + k + 1)
                    elif n == CHUNKS[i]:
                        pe.wait_ge(low_ready, i + 1)
                    mm = nc.tensor.matmul(look_ps[:, i % 2, samples(i)], rows_of_table,
                                          onehot[0:ROWS, i % MADE, k, samples(i)],
                                          start=(n == 0), stop=(n == len(products) - 1))
                mm.then_inc(looked, 1)

            def turn_group(t, u):
                pe.wait_ge(turn_saved, t * NGROUPS + (u + 1))
                pe.wait_ge(rows_landed[u], t * (16 * len(GROUPS[u])) + 16 * len(GROUPS[u]))
                for n, i in enumerate(GROUPS[u]):
                    mm = nc.tensor.transpose(turn_ps[:, u % 2, n * P:(n + 1) * P], rows[:, i, :], ident[:])
                mm.then_inc(turned, 1)

            pe.wait_ge(zeros_ready, 1)
            for b in range(2):
                for q in range(0, QB, 4):
                    nc.tensor.matmul(gram_ps[:, b, q * SLOTS:(q + 4) * SLOTS], zeros[:], zeros[:, 0:4 * SLOTS],
                                     start=True, stop=True)
            pe.wait_ge(consts_ready, 3)
            pe.wait_ge(x_landed, 16)
            for i in range(TILES):
                mm = nc.tensor.transpose(turn_ps[:, 0, i * P:(i + 1) * P], x_rows[:, i, :], ident[:])
            mm.then_inc(turned, 1)
            for i in range(NE):
                look_up(i)
                for u in TURN_AFTER.get(i, []):
                    if u == "late":
                        pe.wait_ge(rows_late_landed, 16 * NL)
                        for n in range(NL):
                            mm = nc.tensor.transpose(turn_ps[:, 1, n * P:(n + 1) * P], rows_late[:, n, :], ident[:])
                        mm.then_inc(turned, 1)
                    else:
                        turn_group(0, u)

            def between(t, step, first, last):
                if not last:
                    for u in NEXT_AFTER[step]:
                        turn_group(t + 1, u)
                if first:
                    for i in LATE_AFTER.get(step, []):
                        look_up(i)

            def layer2(done):
                for m in range(N2):
                    for n in range(N1):
                        if m == 0:
                            if n < N1_DVE:
                                pe.wait_ge(h1_saved[0], done * N1_DVE + (n + 1 - N1_DVE))
                            else:
                                pe.wait_ge(h1_saved[1], done)
                        mm = nc.tensor.matmul(look_ps[:, m, 0:P], w2_sb[:, n, m * P:(m + 1) * P],
                                              h1[:, n, :], start=(n == 0), stop=(n == N1 - 1))
                    mm.then_inc(h2_done, 1)

            def layer3(done):
                for m in range(N2):
                    pe.wait_ge(h2_saved[m], done)
                    mm = nc.tensor.matmul(look_ps[0:1, 0, P:2 * P], w3_sb[:, m:m + 1], h2[:, m, :],
                                          start=(m == 0), stop=(m == N2 - 1))
                mm.then_inc(y_done, 1)

            def tile(t, first, last):
                if not first:
                    for u in START_GROUPS[:-1]:
                        turn_group(t, u)
                if not first:
                    pe.wait_ge(h1_saved[0], t * N1_DVE)
                    pe.wait_ge(h1_saved[1], t)
                for n in range(N1):
                    nc.tensor.matmul(mlp_ps[:, n // N1_DVE, h_cols[n % N1_DVE]], w1_sb[:, PAIR_CHUNKS, n * P:(n + 1) * P],
                                     known[:, DENSE, bass.ts(t, P)], start=(n % N1_DVE == 0), stop=False,
                                     skip_group_check=True)
                if last:
                    for _ in range(KEEP_CLOCK):
                        nc.tensor.matmul(look_ps[:, 0, 2 * P:3 * P], zeros[:], zeros[:], start=True, stop=True)
                if not first:
                    turn_group(t, START_GROUPS[-1])
                pe.wait_ge(known_placed, t + 1)
                pe.wait_ge(turn_saved, t * NGROUPS + NGROUPS + 2)
                for b in range(2):
                    for q in range(QB):
                        for j in range(4):
                            v = vecs[:, j * JQ + b * QB + q, :]
                            mm = nc.tensor.matmul(gram_ps[32 * j:32 * j + SLOTS, b, q * SLOTS:(q + 1) * SLOTS],
                                                  v, v, start=True, stop=True)
                mm.then_inc(gram_done, 1)
                if not first:
                    layer2(t)
                between(t, "gram", first, last)
                pe.wait_ge(pairs_packed, t + 1)
                for c in range(PAIR_CHUNKS):
                    mm = nc.tensor.transpose(gram_ps[:, c // 2, (c % 2) * P:(c % 2 + 1) * P],
                                             pairs[:, c * P:(c + 1) * P], ident[:])
                    if c in (1, PAIR_CHUNKS - 1):
                        mm.then_inc(pairs_turned, 1)
                between(t, "pairs", first, last)
                if not first:
                    layer3(t)
                if first:
                    pe.wait_ge(w1_landed, 16)
                for n in range(N1):
                    for c in range(PAIR_CHUNKS):
                        if n == 0 and c % 2 == 0:
                            pe.wait_ge(pairs_saved[c // 2], t + 1)
                        mm = nc.tensor.matmul(mlp_ps[:, n // N1_DVE, h_cols[n % N1_DVE]], w1_sb[:, c, n * P:(n + 1) * P],
                                              pairs_t[:, c, :], start=False, stop=(c == PAIR_CHUNKS - 1),
                                              skip_group_check=True)
                    if n >= N1_DVE - 1:
                        mm.then_inc(h1_done, 1)
                between(t, "layer1", first, last)

            pe.wait_ge(wx_landed, 16)
            tile(0, True, False)
            pe.wait_ge(look_saved, NO)
            pe.wait_ge(w2_landed, 16)
            pe.wait_ge(small_landed, 48)
            with pe.Fori(1, TILES - 1) as t:
                tile(t, False, False)
            tile(TILES - 1, False, True)
            pe.wait_ge(y_saved, TILES - 1)
            layer2(TILES)
            layer3(TILES)

        @block.vector
        def _(dve):
            copy = nc.vector.tensor_copy

            def make_look_up(i):
                dve.wait_ge(wide_landed[i], 16)
                if i >= MADE:
                    dve.wait_ge(looked, i - MADE + 1)
                for k in range(CHUNKS[i]):
                    nc.vector.tensor_scalar(onehot[:, i % MADE, k, samples(i)], ids_wide[:, i % HELD, samples(i)],
                                            row_ids[:, (CHUNKS[i] - 8) // 2, k:k + 1], None, ALU.is_equal
                                            ).then_inc(onehot_ready, 1)
                dve.wait_ge(high_ready, i + 1)
                nc.vector.tensor_tensor(low_of(i), table_of(i), high_of(i).bitcast(F32), ALU.subtract
                                        ).then_inc(low_ready, 1)

            def late_look_ups(step):
                for i in MAKE_BEFORE.get(step, []):
                    make_look_up(i)

            nc.vector.memset(zeros[:], 0.0).then_inc(zeros_ready, 1)
            nc.vector.memset(pairs[:, PAIRS:], 0.0)
            dve.wait_ge(consts_ready, 3)
            for i in range(NE):
                make_look_up(i)

            def save_h2(done):
                dve.wait_ge(h2_done, done * 2 - 1)
                nc.vector.tensor_scalar(h2[:, 0, :], look_ps[:, 0, 0:P], b2_sb[:, 0:1], 0.0, ALU.add,
                                        ALU.max).then_inc(h2_saved[0], 1)

            def tile(t, first, last):
                if first:
                    late_look_ups("dots")
                dve.wait_ge(gram_done, t + 1)
                nc.vector.transpose(dots[:], gram_ps[:, :, 0:QB * SLOTS].rearrange("p h (q g) -> p g h q", g=SLOTS)
                                    ).then_inc(dots_ready, 1)
                dve.wait_ge(dots_ready, t + 1)
                at = 0
                for g, f, dims in PACKS:
                    n = 1
                    for _, _, count in dims:
                        n *= count
                    src = bass.AP(tensor=dots[:].tensor, offset=g * 32 + f,
                                  ap=[[SLOTS * 32, P]] + [[32 * step_g + step_f, count]
                                                          for step_g, step_f, count in dims])
                    names = "abc"[:len(dims)]
                    dst = pairs[:, at:at + n]
                    if len(dims) > 1:
                        dst = dst.rearrange(f"p ({' '.join(names)}) -> p {' '.join(names)}",
                                            **{x: d[2] for x, d in zip(names, dims)})
                    ins = copy(dst, src)
                    at += n
                ins.then_inc(pairs_packed, 1)
                if first:
                    late_look_ups("pairs_t")
                else:
                    save_h2(t)
                dve.wait_ge(pairs_turned, t * 2 + 1)
                copy(pairs_t[:, 0:2, :], gram_ps[:, 0, 0:2 * P].rearrange("p (c b) -> p c b", c=2)
                     ).then_inc(pairs_saved[0], 1)
                if first:
                    late_look_ups("h1")
                dve.wait_ge(h1_done, t * 2 + 1)
                for n in range(N1_DVE):
                    nc.vector.tensor_scalar(h1[:, n, :], mlp_ps[:, 0, h_cols[n]], b1_sb[:, n:n + 1],
                                            0.0, ALU.add, ALU.max).then_inc(h1_saved[0], 1)

            dve.wait_ge(small_landed, 48)
            tile(0, True, False)
            with dve.Fori(1, TILES - 1) as t:
                tile(t, False, False)
            tile(TILES - 1, False, True)
            save_h2(TILES)

        @block.scalar
        def _(act):
            copy = nc.scalar.copy
            wide_dma(act, 0)
            act.dma_start(x_rows[:], x.rearrange("(t p) d -> p t d", p=P)).then_inc(x_landed, 16)

            def spread(bank, n):
                return bank[:, 0:n * P].rearrange("p (s b) -> p b s", b=P)

            def make_high(i):
                act.wait_ge(table_landed[i], 16)
                if i >= HELD:
                    act.wait_ge(looked, i - HELD + 1)
                copy(high_of(i), table_of(i)).then_inc(high_ready, 1)

            def save_look_up(i):
                act.wait_ge(looked, i + 1)
                copy(known[:, slot(i), samples(i)], look_ps[:, i % 2, samples(i)]).then_inc(look_saved, 1)

            def place(t, slots):
                return copy(vecs[:, :, slots], known[:, slots, bass.ts(t, P)].rearrange("p s b -> p b s"))

            def save_group(t, u):
                act.wait_ge(turned, t * NGROUPS + (u + 3))
                copy(vecs[:, :, KNOWN + GROUPS[u].start:KNOWN + GROUPS[u].stop],
                     spread(turn_ps[:, u % 2, :], len(GROUPS[u]))).then_inc(turn_saved, 1)

            make_high(0)
            act.wait_ge(turned, 1)
            copy(known[:, DENSE, :], turn_ps[:, 0, :]).then_inc(turn_saved, 1)
            make_high(1)
            for i in range(NE):
                make_high(i + 2)
                if i == NE - 1:
                    act.wait_ge(look_saved, NE - 1)
                    place(0, slice(0, NE - 1))
                save_look_up(i)
                for u in TURN_AFTER.get(i, []):
                    if u == "late":
                        act.wait_ge(turned, 2)
                        copy(vecs[:, :, NE + 1:KNOWN], spread(turn_ps[:, 1, :], NL)).then_inc(turn_saved, 1)
                    else:
                        save_group(0, u)
            act.wait_ge(turn_saved, 1)
            act.wait_ge(look_saved, NE)
            place(0, slice(NE - 1, NE + 1)).then_inc(known_placed, 1)

            def between(t, step, first, last):
                if not last:
                    for u in NEXT_AFTER[step]:
                        save_group(t + 1, u)
                if first:
                    for i in LATE_AFTER.get(step, []):
                        save_look_up(i)

            def save_h2(done):
                act.wait_ge(h2_done, done * 2)
                nc.scalar.activation(h2[:, 1, :], look_ps[:, 1, 0:P], ACT.Relu,
                                     bias=b2_sb[:, 1:2]).then_inc(h2_saved[1], 1)

            def save_y(t, done):
                act.wait_ge(y_done, done)
                copy(y[:, bass.ts(t, P)], look_ps[0:1, 0, P:2 * P]).then_inc(y_saved, 1)

            def tile(t, first, last):
                if first:
                    for i in range(NE + 2, NO):
                        make_high(i)
                if not first:
                    for u in START_GROUPS:
                        save_group(t, u)
                if not last:
                    act.wait_ge(gram_done, t + 1)
                    if not first:
                        place(t + 1, slice(0, KNOWN)).then_inc(known_placed, 1)
                if not first:
                    save_h2(t)
                between(t, "gram", first, last)
                act.wait_ge(pairs_turned, t * 2 + 2)
                copy(pairs_t[:, 2, :], gram_ps[:, 1, 0:P]).then_inc(pairs_saved[1], 1)
                between(t, "pairs", first, last)
                if not first:
                    save_y(t - 1, t)
                act.wait_ge(h1_done, t * 2 + 2)
                nc.scalar.activation(h1[:, N1_DVE, :], mlp_ps[:, 1, h_cols[0]], ACT.Relu,
                                     bias=b1_sb[:, N1_DVE:N1]).then_inc(h1_saved[1], 1)
                between(t, "layer1", first, last)
                if first:
                    act.wait_ge(look_saved, NO)
                    place(t + 1, slice(0, KNOWN)).then_inc(known_placed, 1)

            act.wait_ge(small_landed, 48)
            tile(0, True, False)
            with act.Fori(1, TILES - 1) as t:
                tile(t, False, False)
            tile(TILES - 1, False, True)
            save_h2(TILES)
            save_y(TILES - 1, TILES)


def kernel(**inputs):
    import numpy as np
    import concourse.bacc as bacc
    from concourse.bass_utils import run_bass_kernel_spmd

    row_of = {}
    for i in range(SLOTS):
        for j in range(i + 1, SLOTS):
            row_of[i, j] = len(row_of)
    order = [row_of[tuple(sorted((SLOT_FIELDS[f], SLOT_FIELDS[g])))] for f, g in pack_order()]
    w1_in = np.asarray(inputs["W_top1"])
    w1 = np.zeros(((PAIR_CHUNKS + 1) * P, H1), w1_in.dtype)
    w1[:PAIRS] = w1_in[np.array(order)]
    w1[PAIR_CHUNKS * P:] = w1_in[PAIRS:]
    ids = np.asarray(inputs["ids"])

    arrays = {
        "ids_gather": ids[:, GATHER_FIELDS],
        "ids_late": ids[:P, LATE_FIELDS],
        "ids_onehot": ids[:, ONEHOT_FIELDS].T.reshape(-1),
        "x": inputs["r_dense_x"],
        "w1": w1.reshape(PAIR_CHUNKS + 1, P, H1).transpose(1, 0, 2).reshape(P, -1),
        "b1": np.asarray(inputs["b_top1"]).reshape(N1, P).T,
        "w2": inputs["W_top2"],
        "b2": np.asarray(inputs["b_top2"]).reshape(N2, P).T,
        "w3": np.asarray(inputs["W_top3"]).reshape(N2, P).T,
    }
    for f in range(FIELDS):
        arrays[f"tbl_{f}"] = inputs[f"tbl_{f}"]
    nc = bacc.Bacc("TRN2", target_bir_lowering=False, num_devices=1)
    given, dram = {}, {}
    for name, a in arrays.items():
        given[f"{name}_dram"] = np.ascontiguousarray(a)
        dram[name] = nc.dram_tensor(f"{name}_dram", given[f"{name}_dram"].shape,
                                    mybir.dt.from_np(given[f"{name}_dram"].dtype), kind="ExternalInput").ap()
    out = nc.dram_tensor("out_dram", (BATCH, 1), F32, kind="ExternalOutput").ap()
    build(nc, dram["ids_gather"], dram["ids_late"], dram["ids_onehot"], dram["x"], [dram[f"tbl_{f}"] for f in range(FIELDS)],
          dram["w1"], dram["b1"], dram["w2"], dram["b2"], dram["w3"], out)
    result = run_bass_kernel_spmd(nc, [given], core_ids=[0])
    return result.results[0]["out_dram"]
```
